# Optimizing a Trainium2 kernel written in Bass

```python
import numpy as np
import jax
import jax.numpy as jnp

def _softmax(x, axis=-1):
    return jax.nn.softmax(x, axis=axis)

def _gelu(x):
    return jax.nn.gelu(x, approximate=True)

def _silu(x):
    return jax.nn.silu(x)

def _sigmoid(x):
    return jax.nn.sigmoid(x)

def _layernorm(x, axis=-1, eps=1e-05):
    m = jnp.mean(x, axis=axis, keepdims=True)
    v = jnp.var(x, axis=axis, keepdims=True)
    return (x - m) / jnp.sqrt(v + eps)

def _scatter_add(tgt, idx, src, axis=0):
    return tgt.at[idx].add(src)

def _segment_sum(src, seg, n):
    return jax.ops.segment_sum(src, seg, n)
kernel_name = 'mk_adaln_d1_jaxref_r4_ba4b26'

def setup_inputs(seed: int=0):
    np.random.seed(seed)
    _w = jnp.asarray

    def _L0_attn_setup():
        import jax, jax.numpy as jnp
        import numpy as np
        NUM_HEADS = 16
        key = jax.random.key(seed)
        k1, k2, k3, k4 = jax.random.split(key, 4)
        B, N, D = (4, 512, 256)
        inputs = jax.random.normal(k1, (B, N, D), dtype=jnp.float32)
        w_in = jax.random.normal(k2, (3 * D, D), dtype=jnp.float32) * D ** (-0.5)
        w_out = jax.random.normal(k3, (D, D), dtype=jnp.float32) * D ** (-0.5)
        b_out = jax.random.normal(k4, (D,), dtype=jnp.float32) * 0.02
        return {'inputs': inputs, 'w_in': w_in, 'w_out': w_out, 'b_out': b_out}
    _L0_attn_in = _L0_attn_setup()

    def _L0_ffn_setup():
        import jax, jax.numpy as jnp
        import numpy as np
        DIM = 256

        def _reference_tuple_inner(x, W_r, W_k, W_v, mu_r, mu_k):
            B, T, C = x.shape
            x_prev = jnp.concatenate([jnp.zeros((B, 1, C), x.dtype), x[:, :-1, :]], axis=1)
            xr = mu_r * x + (1.0 - mu_r) * x_prev
            xk = mu_k * x + (1.0 - mu_k) * x_prev
            r = jax.nn.sigmoid(jnp.einsum('btc,dc->btd', xr, W_r))
            k = jnp.einsum('btc,dc->btd', xk, W_k)
            k_act = jnp.square(jax.nn.relu(k))
            out = r * jnp.einsum('btc,dc->btd', k_act, W_v)
            new_state = x[:, -1, :]
            return (out, new_state)
        key = jax.random.key(seed)
        ks = jax.random.split(key, 6)
        B, T, C = (8, 512, DIM)
        x = jax.random.normal(ks[0], (B, T, C), dtype=jnp.float32)
        s = 1.0 / np.sqrt(C)
        W_r = jax.random.uniform(ks[1], (C, C), jnp.float32, -s, s)
        W_k = jax.random.uniform(ks[2], (C, C), jnp.float32, -s, s)
        W_v = jax.random.uniform(ks[3], (C, C), jnp.float32, -s, s)
        mu_r = jax.random.uniform(ks[4], (C,), jnp.float32)
        mu_k = jax.random.uniform(ks[5], (C,), jnp.float32)
        return {'x': x, 'W_r': W_r, 'W_k': W_k, 'W_v': W_v, 'mu_r': mu_r, 'mu_k': mu_k}
    _L0_ffn_in = _L0_ffn_setup()
    _L0_c = _w((lambda *s: np.random.randn(*s).astype(np.float32) * 0.05)(8, 256))
    _L0_wmod = _w((lambda *s: np.random.randn(*s).astype(np.float32) * 0.05)(256, 6 * 256) * 256 ** (-0.5))
    _d = {'L0_attn_inputs': _L0_attn_in['inputs'], 'L0_attn_w_in': _L0_attn_in['w_in'], 'L0_attn_w_out': _L0_attn_in['w_out'], 'L0_attn_b_out': _L0_attn_in['b_out'], 'L0_ffn_W_r': _L0_ffn_in['W_r'], 'L0_ffn_W_k': _L0_ffn_in['W_k'], 'L0_ffn_W_v': _L0_ffn_in['W_v'], 'L0_ffn_mu_r': _L0_ffn_in['mu_r'], 'L0_ffn_mu_k': _L0_ffn_in['mu_k'], 'L0_c': _L0_c, 'L0_wmod': _L0_wmod}
    _x0 = _d['L0_attn_inputs']
    _d['L0_attn_inputs'] = jax.random.normal(jax.random.fold_in(jax.random.key(seed), 1), (8, 1024, 256), dtype=_x0.dtype)
    del _x0
    return _d

def reference(L0_attn_inputs, L0_attn_w_in, L0_attn_w_out, L0_attn_b_out, L0_ffn_W_r, L0_ffn_W_k, L0_ffn_W_v, L0_ffn_mu_r, L0_ffn_mu_k, L0_c, L0_wmod):

    def _L0_attn_ref(inputs, w_in, w_out, b_out):
        import jax, jax.numpy as jnp
        import numpy as np
        NUM_HEADS = 16
        B, N, D = inputs.shape
        H = NUM_HEADS
        Hd = D // H
        qkv = jnp.einsum('bnd,ed->bne', inputs, w_in)
        q, k, v = jnp.split(qkv, 3, axis=-1)
        q = q.reshape(B, N, H, Hd).transpose(0, 2, 1, 3)
        k = k.reshape(B, N, H, Hd).transpose(0, 2, 1, 3)
        v = v.reshape(B, N, H, Hd).transpose(0, 2, 1, 3)
        scores = jnp.einsum('bhqd,bhkd->bhqk', q, k) * Hd ** (-0.5)
        causal = jnp.triu(jnp.ones((N, N), dtype=bool), k=1)
        scores = jnp.where(causal, -jnp.inf, scores)
        attn = jax.nn.softmax(scores, axis=-1)
        out = jnp.einsum('bhqk,bhkd->bhqd', attn, v)
        out = out.transpose(0, 2, 1, 3).reshape(B, N, D)
        return jnp.einsum('bnd,ed->bne', out, w_out) + b_out

    def _L0_ffn_ref(x, W_r, W_k, W_v, mu_r, mu_k):
        import jax, jax.numpy as jnp
        import numpy as np
        DIM = 256

        def _reference_tuple_inner(x, W_r, W_k, W_v, mu_r, mu_k):
            B, T, C = x.shape
            x_prev = jnp.concatenate([jnp.zeros((B, 1, C), x.dtype), x[:, :-1, :]], axis=1)
            xr = mu_r * x + (1.0 - mu_r) * x_prev
            xk = mu_k * x + (1.0 - mu_k) * x_prev
            r = jax.nn.sigmoid(jnp.einsum('btc,dc->btd', xr, W_r))
            k = jnp.einsum('btc,dc->btd', xk, W_k)
            k_act = jnp.square(jax.nn.relu(k))
            out = r * jnp.einsum('btc,dc->btd', k_act, W_v)
            new_state = x[:, -1, :]
            return (out, new_state)
        return _reference_tuple_inner(x, W_r, W_k, W_v, mu_r, mu_k)[0]
    x = L0_attn_inputs
    mod = (_silu(L0_c) @ L0_wmod).reshape(L0_c.shape[0], 6, 1, -1)
    sa, ca, ga, sb, cb, gb = (mod[:, 0], mod[:, 1], mod[:, 2], mod[:, 3], mod[:, 4], mod[:, 5])
    ga = (2 * (ga >= 0) - 1) * jnp.maximum(jnp.abs(ga), 0.25)
    gb = (2 * (gb >= 0) - 1) * jnp.maximum(jnp.abs(gb), 0.25)
    h = _layernorm(x, axis=-1) * (1 + ca) + sa
    x = x + ga * _L0_attn_ref(h, L0_attn_w_in, L0_attn_w_out, L0_attn_b_out)
    h = _layernorm(x, axis=-1) * (1 + cb) + sb
    x = x + gb * _L0_ffn_ref(h, L0_ffn_W_r, L0_ffn_W_k, L0_ffn_W_v, L0_ffn_mu_r, L0_ffn_mu_k)
    return x

_drawn_inputs = setup_inputs


def setup_inputs(seed=0):
    import zlib

    import numpy as np

    out = dict(_drawn_inputs(seed))
    spreads = {}
    factors = {'L0_attn_b_out': 25.454,
     'L0_ffn_W_r': 8.0,
     'L0_ffn_W_k': 3.02,
     'L0_ffn_W_v': 2.769,
     'L0_ffn_mu_r': 8.0,
     'L0_ffn_mu_k': 5.006}
    for name, (base, spread) in spreads.items():
        noise = np.random.default_rng([zlib.crc32(name.encode()), seed]).standard_normal(out[name].shape)
        drawn = base * np.exp(spread * noise) if base else spread * noise
        out[name] = jnp.asarray(drawn.astype(out[name].dtype))
    for name, factor in factors.items():
        out[name] = (out[name] * factor).astype(out[name].dtype)
    return out
```

```python
from contextlib import ExitStack

import concourse.bass as bass
from concourse import mybir

F32 = mybir.dt.float32
F32R = mybir.dt.float32r
BF16 = mybir.dt.bfloat16
I32 = mybir.dt.int32
ALU = mybir.AluOpType
ACT = mybir.ActivationFunctionType
AX_X = mybir.AxisListType.X

P = 128
B, N, D, H = 8, 1024, 256, 16
HD = D // H
KC = D // P
NT = N // P
G = 4
HALF = 512
QT = 256
STEPS = 12
EPS = 1e-5
SCALE = float(HD) ** -0.5
MASKED = -3.0e38

Q_PARTS = (0, 0, 0, 1, 1, 2)
K_PARTS = (0, 1, 2, 0, 1, 0)
ROWS = len(Q_PARTS) * HD
MROWS = 3
FILL = 2 * len(Q_PARTS) * 16

COL_STEPS = [(P * j, HALF, j) for j in range(4)] + [(max(HALF, P * j), N, j) for j in range(NT)]
DIAGONAL = [t for t, (q0, _, j) in enumerate(COL_STEPS) if q0 == P * j]
COL_HEADS = [{1: 4, 2: 2, 3: 1, 4: 1}[(q1 - q0) // P] for q0, q1, _ in COL_STEPS]
COL_FIRST = [sum(G // n for n in COL_HEADS[:t]) for t in range(STEPS + 1)]
COLS = COL_FIRST[STEPS]


MT0_AFTER = 3


def row_units():
    units = []
    for i in range(NT):
        spans = [(0, P * (i + 1))] if i < 4 else [(0, HALF), (HALF, P * (i + 1))]
        for second, (k0, k1) in enumerate(spans):
            width = k1 - k0
            heads = min(G, HALF // width)
            heads = 1 if heads == 3 else heads
            units += [(i, range(h, h + heads), k0, k1, second) for h in range(0, G, heads)]
    return units


ROW_UNITS = row_units()
FIRST_HALF = sum(1 for u in ROW_UNITS if u[0] < 4)
MT0 = FIRST_HALF + MT0_AFTER
ORDER = ROW_UNITS[:MT0] + ["mt0"] + ROW_UNITS[MT0:]
MT1 = len(ORDER)
UNITS = MT1 + 1
PER_STEP = [2, 3, 3, 3, 3, 4, 4, 5, 5, 4, 2, 1]
assert sum(PER_STEP) == len(ORDER)
V_STEPS, QK_STEPS, T_STEPS = (0, 1, 2, 3), (4, 6, 7, 8), (4, 6, 8, 10)
BACK_UNITS = ("out", "norm", "recept", "key", "value")
BACK_STEPS = dict(zip(BACK_UNITS, (2, 5, 9, 10, 13)))
BACK_END = 15
TAIL_LAG = 5

W_QK, W_V, W_O, W_R, W_K, W_F = 0, 1024, 1536, 2048, 2560, 3072
W_ALL = 3584


def build(nc, x, w_in_t, w_out_t, b_out, w_r_t, w_k_t, w_v_t, mu_r, mu_k, c_t, wmod, out):
    x_tiles = x.rearrange("b (t p) c -> b p t c", p=P)
    out_tiles = out.rearrange("b (t p) c -> b p t c", p=P)

    def wait(eng, sem, value):
        if not (isinstance(value, int) and value <= 0):
            eng.wait_ge(sem, value)

    with ExitStack() as ctx:
        def sb(name, shape, dt=F32):
            return ctx.enter_context(nc.sbuf_tensor(name, shape, dt))

        def ps(name, shape, dt=F32):
            return ctx.enter_context(nc.psum_tensor(name, shape, dt))

        def sem(name):
            return ctx.enter_context(nc.semaphore(name))

        passed = {name: sem(f"passed_{name}") for name in ("sp", "pool", "dve")}

        def wait_apart(eng, name, semaphore, value):
            if not (isinstance(value, int) and value <= 0):
                eng.wait_ge(semaphore, value)
                eng.sem_inc(passed[name], 1)

        col_ps = [ps(f"col_ps{i}", [P, HALF]) for i in range(3)]
        row_ps = [ps(f"row_ps{i}", [P, HALF]) for i in range(3)]
        val_ps = ps("val_ps", [P, HALF])
        dense_ps = ps("dense_ps", [P, 2, QT])
        dense_flat = dense_ps[:].rearrange("p a n -> p (a n)")

        w_hi = sb("w_hi", [P, W_ALL], F32R)
        w_lo = sb("w_lo", [P, W_ALL], F32R)
        ident = sb("ident", [P, P])
        ident_bf = sb("ident_bf", [P, P], BF16)
        causal = sb("causal", [P, P], BF16)
        zero_col = sb("zero_col", [P, 1])
        mus = sb("mus", [P, 2, KC])
        neg_half = sb("neg_half", [P, 2])
        mod_t = sb("mod_t", [P, B * 8])
        mod_front = sb("mod_front", [P, 4])
        mod_back = sb("mod_back", [P, 4])
        gates_att = sb("gates_att", [P, 2, D])
        gates_mix = sb("gates_mix", [P, D])

        q_stack = [sb(f"q_stack{i}", [ROWS + MROWS, G, N], BF16) for i in range(2)]
        k_stack = [sb(f"k_stack{i}", [ROWS + MROWS, G, N], BF16) for i in range(2)]
        q_parts = [sb(f"q_part{i}", [P, N], BF16) for i in range(3)]
        k_parts = [sb(f"k_part{i}", [P, N], BF16) for i in range(3)]
        qk_rest = sb("qk_rest", [P, HALF])
        v_ones = sb("v_ones", [P, NT, H, HD, 2])
        weights = sb("weights", [P, 2, G, HALF])
        max_a = sb("max_a", [P, NT, G])
        max_b = sb("max_b", [P, 4, G])
        max_rest = sb("max_rest", [P, 4, G])
        max_parts = [sb(f"max_parts{i}", [P, 4, 3 * G], BF16) for i in range(2)]
        max_rows = [sb(f"max_rows{i}", [3 * G, HALF], BF16) for i in range(2)]
        val_out = [sb(f"val_out{i}", [P, HALF]) for i in range(2)]
        att = sb("att", [P, KC, N])
        sums = [sb(f"sums{i}", [P, G * HALF // 32]) for i in range(2)]
        recips = sb("recips", [P, KC, HALF])
        att_n = sb("att_n", [P, KC, N])
        o_hi = sb("o_hi", [P, KC, QT], F32R)
        o_lo = sb("o_lo", [P, KC, QT], F32R)

        xa = sb("xa", [P, NT, D])
        stats_a = sb("stats_a", [P, 2, 6])
        mv_a = sb("mv_a", [P, 2, 2])
        var_a = sb("var_a", [P, 2])
        rstd_a = sb("rstd_a", [P, 2])
        xn_a = sb("xn_a", [P, 2, D])
        h_full = sb("h_full", [P, KC, QT])
        h_hi = sb("h_hi", [P, KC, N], F32R)
        h_lo = sb("h_lo", [P, KC, N], F32R)

        xq = [sb(f"xq{i}", [P, 2, D]) for i in range(2)]
        gated = sb("gated", [P, 2, D])
        mix_out = sb("mix_out", [P, 2, D])
        stats_c = sb("stats_c", [P, 2, 6])
        mv_c = sb("mv_c", [P, 2, 2])
        var_c = sb("var_c", [P, 2])
        rstd_c = sb("rstd_c", [P, 2])
        xn_c = sb("xn_c", [P, 2, D])
        h2 = [sb(f"h2_{i}", [P, KC, 1 + QT]) for i in range(2)]
        h2_diff = sb("h2_diff", [P, KC, QT])
        mixed = sb("mixed", [P, 2, KC, QT])
        mix_hi = sb("mix_hi", [P, 2, KC, QT], F32R)
        mix_lo = sb("mix_lo", [P, 2, KC, QT], F32R)
        recept = sb("recept", [P, 2, D])
        k_relu = sb("k_relu", [P, KC, QT])
        k_sq = sb("k_sq", [P, KC, QT])
        k_hi = sb("k_hi", [P, KC, QT], F32R)
        k_lo = sb("k_lo", [P, KC, QT], F32R)

        xq_tail = [weights[:, 0, i, :].rearrange("p (a d) -> p a d", a=2) for i in range(4)]

        gate_rows = nc.dram_tensor("gate_rows", (B, 3 * D), F32, kind="Internal").ap()
        recip_rows = [nc.dram_tensor(f"recip_rows{i}", (H, HALF), F32, kind="Internal").ap() for i in range(2)]

        w_loaded = sem("w_loaded")
        small_loaded = sem("small_loaded")
        consts_zero = sem("consts_zero")
        consts_done = sem("consts_done")
        w_hi_done = sem("w_hi_done")
        setup_chain = sem("setup_chain")
        tanh_done = sem("tanh_done")
        silu_done = sem("silu_done")
        mod_ready = sem("mod_ready")
        gates_done = sem("gates_done")
        gate_stored = sem("gate_stored")
        setup_done = sem("setup_done")
        ones_done = sem("ones_done")
        stack_filled = [[sem(f"stack_filled{i}_half{h}") for h in range(2)] for i in range(2)]
        rows_ready = sem("rows_ready")
        max_done = sem("max_done")
        max_chain = sem("max_chain")
        max_split = sem("max_split")
        max_placed = [sem(f"max_placed{i}") for i in range(2)]
        cols_ready = sem("cols_ready")
        exp_done = sem("exp_done")
        sel_done = sem("sel_done")
        val_done = sem("val_done")
        val_copied = sem("val_copied")
        att_placed = [sem(f"att_placed{i}") for i in range(2)]
        recip_done = sem("recip_done")
        recip_stored = [sem(f"recip_stored{i}") for i in range(2)]
        recip_in = [sem(f"recip_in{i}") for i in range(2)]
        att_done = sem("att_done")
        xa_in = sem("xa_in")
        mod_a_done = sem("mod_a_done")
        stats_a_done = sem("stats_a_done")
        mv_a_done = sem("mv_a_done")
        var_a_done = sem("var_a_done")
        rstd_a_done = sem("rstd_a_done")
        xn_a_done = sem("xn_a_done")
        kinds = ("transposed", "qk", "v") + BACK_UNITS
        ready = {k: sem(f"ready_{k}") for k in kinds}
        free = {k: sem(f"free_{k}") for k in kinds}
        h_lo_done = sem("h_lo_done")
        part1_done = sem("part1_done")
        part2_done = sem("part2_done")
        parts_done = sem("parts_done")
        gates_att_in = sem("gates_att_in")
        gates_mix_in = sem("gates_mix_in")
        xq_tail_in = [sem(f"xq_tail_in{i}") for i in range(4)]
        out_stored_tail = sem("out_stored_tail")
        xq_in = [sem(f"xq_in{i}") for i in range(2)]
        mod_c_done = sem("mod_c_done")
        xb_done = sem("xb_done")
        o_hi_done = sem("o_hi_done")
        o_lo_done = sem("o_lo_done")
        x1_done = sem("x1_done")
        stats_c_done = sem("stats_c_done")
        mv_c_done = sem("mv_c_done")
        var_c_done = sem("var_c_done")
        rstd_c_done = sem("rstd_c_done")
        xn_c_done = sem("xn_c_done")
        prev_col_done = sem("prev_col_done")
        diff_done = sem("diff_done")
        mixed_done = sem("mixed_done")
        mix_hi_done = sem("mix_hi_done")
        mix_lo_done = sem("mix_lo_done")
        relu_done = sem("relu_done")
        k_hi_done = sem("k_hi_done")
        k_lo_done = sem("k_lo_done")
        scaled_done = sem("scaled_done")
        out_done = sem("out_done")
        out_stored = [sem(f"out_stored{i}") for i in range(2)]

        w_raw = v_ones[:].rearrange("p t h d a -> p (t h d a)")[:, 0:W_ALL]
        wmod_sb = weights[:].rearrange("p a h n -> p (a h n)")[:, 0:KC * 6 * D].rearrange("p (k n) -> p k n", k=KC)
        c_sb = gated[:, 0, 0:KC * B]
        c_tanh = gated[:, 0, 32:32 + KC * B]
        c_silu = gated[:, 0, 64:64 + KC * B]
        gate_val = xn_c[0:B, :, :].rearrange("p a n -> p (a n)")
        gate_abs = mixed[0:B, 0].rearrange("p a n -> p (a n)")
        gate_sgn = mixed[0:B, 1].rearrange("p a n -> p (a n)")
        b_rows = k_relu[0:B, 0, 0:D]
        gate_out = att_n[0:B].rearrange("p k n -> p (k n)")[:, 0:3 * D].rearrange("p (a n) -> p a n", a=3)

        def attends(kind):
            return kind in ("start", "second", "mid", "last")

        def fronts(kind):
            return kind in ("first", "start", "second", "mid")

        def backs(kind):
            return kind in ("second", "mid", "last", "drain")

        def has_rows(kind, s):
            return fronts(kind) if s == G - 1 else attends(kind)

        def has_late(kind, s):
            return backs(kind) if s == 0 else attends(kind)

        def pipeline(eng, body):
            body(-1, "first")
            body(0, "start")
            body(1, "second")
            with eng.Fori(2, B - 1) as b:
                body(b, "mid")
            body(B - 1, "last")
            body(B, "drain")

        def timeline(b, kind):
            if kind == "drain":
                for t in range((G - 1) * TAIL_LAG + BACK_END):
                    at = [(b - 1, G - 1, t + STEPS)] + [(b, s, t - TAIL_LAG * s) for s in range(G)]
                    yield 0, t, [(bb, s, u) for bb, s, u in at if 0 <= u < BACK_END]
                return
            for s in range(G):
                for t in range(STEPS):
                    at = []
                    if s > 0 and backs(kind):
                        at.append((b, s - 1, t + STEPS))
                    if s == 0 and kind in ("mid", "last"):
                        at.append((b - 1, G - 1, t + STEPS))
                    if backs(kind):
                        at.append((b, s, t))
                    yield s, t, [(bb, ss, u) for bb, ss, u in at if u < BACK_END]

        def exp_index(b, s, c):
            return b * (COLS * G) + (COLS * s + c)

        def bank_of(position, period):
            if position >= 3:
                return position % 3, 3
            last = max(p for p in range(period) if p % 3 == position)
            return position, position + period - last

        def val_index(b, s, t):
            return b * (STEPS * G) + (STEPS * s + t)

        def unit_index(b, s, u):
            return b * (UNITS * G) + (UNITS * (s + 1) + u)

        def quarters(b, s):
            return b * G + (s - G)

        def front_unit(b, kind, s, t):
            if s == 0 and attends(kind):
                if t in V_STEPS:
                    k = V_STEPS.index(t)
                    return "v", k, b * 4 + (k + 1)
                if t in QK_STEPS:
                    k = QK_STEPS.index(t)
                    return "qk", 4 + k, b * 8 + (4 + k + 1)
            if s == 1 and fronts(kind) and t in T_STEPS:
                k = T_STEPS.index(t)
                return "transposed", k, b * 4 + (4 + k + 1)
            if s == 2 and fronts(kind) and t in QK_STEPS:
                k = QK_STEPS.index(t)
                return "qk", k, b * 8 + (8 + k + 1)
            return None

        def back_unit(bb, s, u):
            for name, step in BACK_STEPS.items():
                if u == step:
                    return name, quarters(bb, s) + 1
            return None

        def dense_units(b, kind):
            units = []
            for s, t, at in timeline(b, kind):
                f = front_unit(b, kind, s, t)
                if f:
                    units.append((s, t, f[0], f[2]))
                for item in at:
                    u = back_unit(*item)
                    if u:
                        units.append((s, t, *u))
            return units

        BEFORE = {"start": "first", "second": "start", "mid": "second", "last": "mid", "drain": "last"}

        def gaps(t):
            first, n = sum(PER_STEP[:t]), PER_STEP[t]
            out = [[] for _ in range(5)]
            for k in range(n):
                out[k * 5 // n].append(first + k)
            return out

        def residual(bb, s):
            return xq_tail[s] if isinstance(bb, int) and bb == B else xq[s % 2][:]

        block = ctx.enter_context(nc.Block())

        @block.sync
        def _(sp):
            for ap, at, n in ((w_in_t[:, 0:512], W_QK, 512), (w_in_t[:, 512:768], W_V, 256), (w_out_t, W_O, 256),
                              (w_r_t, W_R, 256), (w_k_t, W_K, 256), (w_v_t, W_F, 256)):
                sp.dma_start(w_raw[:, at:at + KC * n].rearrange("p (k n) -> p k n", k=KC),
                             ap.rearrange("(k p) n -> p k n", p=P)).then_inc(w_loaded, 16)
            sp.dma_start(wmod_sb, wmod.rearrange("(k p) n -> p k n", p=P)).then_inc(small_loaded, 16)
            sp.dma_start(c_sb.rearrange("p (k b) -> p k b", k=KC),
                         c_t.rearrange("(k p) b -> p k b", p=P)).then_inc(small_loaded, 16)
            with nc.allow_non_contiguous_dma("two short columns"):
                sp.dma_start(mus[:, 0, :], mu_r.rearrange("(k p) -> p k", p=P)).then_inc(small_loaded, 16)
                sp.dma_start(mus[:, 1, :], mu_k.rearrange("(k p) -> p k", p=P)).then_inc(small_loaded, 16)
            sp.dma_start(b_rows, b_out.rearrange("(a n) -> a n", a=1).partition_broadcast(B)
                         .rearrange("q a n -> q (a n)")).then_inc(small_loaded, 16)
            sp.dma_start(xa[:], x_tiles[0:1]).then_inc(xa_in, 16)
            sp.wait_ge(gates_done, 1)
            sp.dma_start(gate_rows, gate_out.rearrange("p a n -> p (a n)")).then_inc(gate_stored, 16)
            sp.wait_ge(gate_stored, 16)
            sp.wait_ge(setup_done, 3)

            def hold(semaphore, value):
                wait_apart(sp, "sp", semaphore, value)

            def fill_stacks(b, s, half, sides):
                buf = s % 2
                hold(cols_ready, exp_index(b, s - 2, COLS if half else COL_FIRST[8]))
                hold(parts_done, b * 8 + (8 * (s // 4) + 4 * (s % 4 // 2) + 2 * (half + 1)))
                lo = 64 * (s % 2)
                cols = slice(HALF * half, HALF * (half + 1))
                for side in sides:
                    stack, parts, which = ((q_stack, q_parts, Q_PARTS), (k_stack, k_parts, K_PARTS))[side]
                    for r, part in enumerate(which):
                        sp.dma_start(stack[buf][HD * r:HD * (r + 1), :, cols],
                                     parts[part][lo:lo + 64, cols]).then_inc(stack_filled[buf][half], 16)

            def place_values(b, s, half):
                hold(val_copied, b * (2 * G) + (2 * s + half + 1))
                cols = slice(HALF * half, HALF * (half + 1))
                sp.dma_start(att[64 * (s % 2):64 * (s % 2) + 64, s // 2, cols],
                             val_out[half][0:P:2, :]).then_inc(att_placed[half], 16)
                sp.dma_start(sums[half][32 * s:32 * s + 32, :],
                             val_out[half][1:P:32, :]).then_inc(att_placed[half], 16)

            def spread_recips(b, half):
                hold(recip_done, b * 2 + (half + 1))
                sp.dma_start(recip_rows[half].rearrange("h n -> (h n)").rearrange("(p n) -> p n", p=P),
                             sums[half][:]).then_inc(recip_stored[half], 16)
                hold(recip_stored[half], b * 16 + 16)
                hold(att_done, b * 2 + half)
                for c in range(KC):
                    rows = recip_rows[half][8 * c:8 * c + 1, :]
                    sp.dma_start(recips[:, c, :], bass.AP(tensor=rows.tensor, offset=rows.offset,
                                                          ap=[[HALF, 8], [0, HD], [1, HALF]])
                                 ).then_inc(recip_in[half], 16)

            def load_residual(b, s):
                if isinstance(b, int) and b == B:
                    hold(val_done, val_index(b, 0, 0) - 1)
                    sp.dma_start(xq_tail[s], x_tiles[b - 1, :, 2 * s:2 * s + 2, :]).then_inc(xq_tail_in[s], 16)
                else:
                    hold(out_stored[s % 2], (b * 2 + (s // 2 - 2)) * 16)
                    sp.dma_start(xq[s % 2][:], x_tiles[bass.ds(b - 1, 1), :, 2 * s:2 * s + 2, :]
                                 ).then_inc(xq_in[s % 2], 16)

            def load_gates(b):
                hold(x1_done, quarters(b, 0))
                sp.dma_start(gates_att[:].rearrange("p a n -> p (a n)"),
                             gate_rows[bass.ds(b - 1, 1), 0:2 * D].partition_broadcast(P)).then_inc(gates_att_in, 16)

            def load_mix_gate(b):
                hold(out_done, quarters(b, 0))
                sp.dma_start(gates_mix[:], gate_rows[bass.ds(b - 1, 1), 2 * D:3 * D].partition_broadcast(P)
                             ).then_inc(gates_mix_in, 16)

            def body(b, kind):
                for s in range(1 if kind == "drain" else G):
                    if has_rows(kind, s):
                        fill_stacks(b, s + 1, 1, (0,))
                    if backs(kind) and s == 0:
                        load_gates(b)
                    if backs(kind):
                        for quarter in range(G) if kind == "drain" else [s]:
                            load_residual(b, quarter)
                    if has_late(kind, s):
                        if s == 1:
                            hold(att_done, b * 2)
                        if s == 0:
                            place_values(b - 1, G - 1, 1)
                        else:
                            place_values(b, s - 1, 1)
                    if has_rows(kind, s) and not attends(kind):
                        fill_stacks(b, s + 1, 1, (1,))
                    if fronts(kind) and attends(kind) and s == 0:
                        hold(xn_a_done, b * 4 + 4)
                        sp.dma_start(xa[:], x_tiles[bass.ds(b + 1, 1)]).then_inc(xa_in, 16)
                    if attends(kind):
                        hold(max_done, unit_index(b, s - 1, MT1) + 1)
                        for part in range(3):
                            sp.dma_start(q_stack[s % 2][ROWS + part:ROWS + part + 1, :, HALF:N],
                                         max_rows[1][G * part:G * part + G, :]).then_inc(max_placed[1], 16)
                        if has_rows(kind, s):
                            fill_stacks(b, s + 1, 1, (1,))
                    if backs(kind) and s == 0:
                        load_mix_gate(b)
                        spread_recips(b - 1, 1)
                    if attends(kind):
                        if s == 0:
                            hold(att_done, b * 2 - 1)
                        place_values(b, s, 0)
                    if has_rows(kind, s):
                        hold(max_done, unit_index(b, s, MT0) + 1)
                        for part in range(3):
                            sp.dma_start(q_stack[(s + 1) % 2][ROWS + part:ROWS + part + 1, :, 0:HALF],
                                         max_rows[0][G * part:G * part + G, :]).then_inc(max_placed[0], 16)
                    if fronts(kind) if s >= 2 else attends(kind):
                        fill_stacks(b, s + 2, 0, (0, 1))
                    if attends(kind) and s == G - 1:
                        spread_recips(b, 0)

            pipeline(nc.sync, body)
            for i in range(2):
                sp.wait_ge(out_stored[i], 16 * 2 * (B - 1))
            sp.wait_ge(out_stored_tail, 16 * G)

        @block.gpsimd
        def _(pool):
            nc.gpsimd.memset(ident[:], 0.0)
            nc.gpsimd.memset(ident_bf[:], 0.0)
            nc.gpsimd.memset(causal[:], 0.0)
            nc.gpsimd.memset(neg_half[:], -0.5).then_inc(consts_zero, 1)
            pool.wait_ge(consts_zero, 1)
            for t in (ident, ident_bf):
                nc.gpsimd.affine_select(out=t[:], in_=t[:], compare_op=ALU.not_equal, fill=1.0, base=0,
                                        pattern=[[-1, P]], channel_multiplier=1)
            nc.gpsimd.affine_select(out=causal[:], in_=causal[:], compare_op=ALU.is_ge, fill=MASKED, base=0,
                                    pattern=[[-1, P]], channel_multiplier=1).then_inc(consts_done, 1)
            pool.wait_ge(consts_done, 1)
            pool.wait_ge(setup_done, 3)
            nc.gpsimd.memset(v_ones[:], 1.0).then_inc(ones_done, 1)
            pool.wait_ge(ones_done, 1)

            def rstd(var, mv, out_t, mv_done, var_done, rstd_done, count):
                wait_apart(pool, "pool", mv_done, count)
                nc.gpsimd.tensor_scalar(var[:], mv[:, :, 1], EPS, None, ALU.add).then_inc(var_done, 1)
                pool.wait_ge(var_done, count)
                nc.gpsimd.tensor_tensor(out_t[:], var[:], neg_half[:], ALU.pow).then_inc(rstd_done, 1)

            def select(b, s, t):
                wait_apart(pool, "pool", exp_done, exp_index(b, s, COL_FIRST[t + 1]))
                w = weights[:, t % 2, :, 0:P]
                nc.gpsimd.affine_select(out=w, in_=w, compare_op=ALU.is_ge, fill=0.0, base=0,
                                        pattern=[[0, G], [1, P]], channel_multiplier=-1).then_inc(sel_done, 1)

            def front(b, kind, s, t):
                unit = front_unit(b, kind, s, t - 1)
                if unit and unit[0] == "qk":
                    _, k, count = unit
                    side = (q_parts, k_parts)[k % 2]
                    cols = slice(HALF * (k % 4 // 2), HALF * (k % 4 // 2 + 1))
                    wait_apart(pool, "pool", free["qk"], count)
                    nc.gpsimd.tensor_copy(side[1][:, cols], qk_rest[:]).then_inc(part2_done, 1)
                    pool.wait_ge(part2_done, count)
                    nc.gpsimd.tensor_tensor(side[2][:, cols], qk_rest[:], side[1][:, cols],
                                            ALU.subtract).then_inc(parts_done, 1)
                if unit and unit[0] == "transposed":
                    _, k, count = unit
                    cols = slice(QT * k, QT * (k + 1))
                    pool.wait_ge(free["transposed"], count)
                    nc.gpsimd.tensor_tensor(h_lo[:, :, cols], h_full[:], h_hi[:, :, cols].bitcast(F32),
                                            ALU.subtract).then_inc(h_lo_done, 1)
                if s == 1 and fronts(kind) and t + 2 in T_STEPS:
                    k = T_STEPS.index(t + 2)
                    rstd(var_a, mv_a, rstd_a, mv_a_done, var_a_done, rstd_a_done, b * 4 + (4 + k + 1))

            def back(b, s, u):
                q = quarters(b, s)
                tail = isinstance(b, int) and b == B
                xr = residual(b, s)
                if u == 1:
                    if tail:
                        pool.wait_ge(xq_tail_in[s], 16)
                    else:
                        pool.wait_ge(xq_in[s % 2], (b * 2 + (s // 2 - 1)) * 16)
                    if s == 0:
                        pool.wait_ge(gates_att_in, b * 16)
                    gb = gates_att[:, 1:2, :].broadcast_to([P, 2, D])
                    nc.gpsimd.tensor_tensor(xr, xr, gb, ALU.add).then_inc(xb_done, 1)
                    pool.wait_ge(o_hi_done, q + 1)
                    nc.gpsimd.tensor_tensor(o_lo[:], att_n[:, :, QT * s:QT * (s + 1)], o_hi[:].bitcast(F32),
                                            ALU.subtract).then_inc(o_lo_done, 1)
                if u == 4:
                    rstd(var_c, mv_c, rstd_c, mv_c_done, var_c_done, rstd_c_done, q + 1)
                if u == 6:
                    now, before = h2[s % 2], h2[1 - s % 2]
                    wait_apart(pool, "pool", mixed_done, q * 2)
                    if s == 0:
                        nc.gpsimd.memset(now[:, :, 0:1], 0.0).then_inc(prev_col_done, 1)
                    else:
                        nc.gpsimd.tensor_copy(now[:, :, 0:1], before[:, :, QT:QT + 1]).then_inc(prev_col_done, 1)
                    pool.wait_ge(prev_col_done, q + 1)
                    pool.wait_ge(free["norm"], q + 1)
                    nc.gpsimd.tensor_tensor(h2_diff[:], now[:, :, 1:1 + QT], now[:, :, 0:QT],
                                            ALU.subtract).then_inc(diff_done, 1)
                if u == 8:
                    wait(pool, ready["key"], q)
                    for m in range(2):
                        pool.wait_ge(mix_hi_done, q * 2 + (m + 1))
                        nc.gpsimd.tensor_tensor(mix_lo[:, m], mixed[:, m], mix_hi[:, m].bitcast(F32),
                                                ALU.subtract).then_inc(mix_lo_done, 1)
                if u == 11:
                    pool.wait_ge(k_hi_done, q + 1)
                    nc.gpsimd.tensor_tensor(k_lo[:], k_sq[:], k_hi[:].bitcast(F32), ALU.subtract
                                            ).then_inc(k_lo_done, 1)
                if u == 14:
                    if s == 0:
                        pool.wait_ge(gates_mix_in, b * 16)
                    pool.wait_ge(free["value"], q + 1)
                    gh = gates_mix[:].rearrange("p (a n) -> p a n", a=1).broadcast_to([P, 2, D])
                    nc.gpsimd.tensor_tensor(mix_out[:], mix_out[:], gh, ALU.mult).then_inc(scaled_done, 1)
                    pool.wait_ge(scaled_done, q + 1)
                    nc.gpsimd.tensor_tensor(xr, xr, mix_out[:], ALU.add).then_inc(out_done, 1)
                    pool.wait_ge(out_done, q + 1)
                    nc.gpsimd.dma_start(out_tiles[bass.ds(b - 1, 1), :, 2 * s:2 * s + 2, :], xr
                                        ).then_inc(out_stored_tail if tail else out_stored[s % 2], 16)

            def body(b, kind):
                for s, t, at in timeline(b, kind):
                    if attends(kind) and t in DIAGONAL:
                        select(b, s, t)
                    front(b, kind, s, t)
                    for item in at:
                        back(*item)

            pipeline(nc.gpsimd, body)

        @block.scalar
        def _(act):
            act.wait_ge(w_loaded, 96)
            nc.scalar.activation(w_hi[:], w_raw, ACT.Copy).then_inc(w_hi_done, 1)
            act.wait_ge(small_loaded, 80)
            nc.scalar.activation(c_tanh, c_sb, ACT.Tanh, scale=0.5).then_inc(tanh_done, 1)
            act.wait_ge(setup_done, 3)

            def exps(b, s, t, c):
                q0, q1, _ = COL_STEPS[t]
                n = COL_HEADS[t]
                h = (c - COL_FIRST[t]) * n
                act.wait_ge(cols_ready, exp_index(b, s, c) + 1)
                if h == 0:
                    wait(act, val_done, val_index(b, s, t) - 1)
                bank, _ = bank_of(COLS * s + c, COLS * G)
                nc.scalar.activation(weights[:, t % 2, h:h + n, 0:q1 - q0],
                                     col_ps[bank][:, 0:n * (q1 - q0)].rearrange("p (h q) -> p h q", h=n),
                                     ACT.Exp, scale=SCALE).then_inc(exp_done, 1)

            def copy_values(b, s, half):
                act.wait_ge(val_done, val_index(b, s, 12 if half else 4))
                wait(act, att_placed[half], (b * G + s) * 32)
                nc.scalar.activation(val_out[half][:], val_ps[:], ACT.Copy).then_inc(val_copied, 1)

            def front(b, kind, s, t):
                unit = front_unit(b, kind, s, t)
                if not unit:
                    return
                name, k, count = unit
                act.wait_ge(ready[name], count)
                if name == "v":
                    if k == 0:
                        wait(act, val_done, val_index(b, 0, 0))
                    nc.scalar.activation(v_ones[:, 2 * k:2 * k + 2, :, :, 0],
                                         dense_ps[:].rearrange("p a (h d) -> p a h d", h=H), ACT.Copy
                                         ).then_inc(free["v"], 1)
                if name == "qk":
                    if k % 4 == 0:
                        for i in range(2):
                            for half in range(2):
                                wait(act, stack_filled[i][half], (b * 2 + (1 if s == 0 else 2)) * FILL)
                    side, half = (q_parts, k_parts)[k % 2], k % 4 // 2
                    nc.scalar.activation(side[0][:, HALF * half:HALF * (half + 1)], dense_flat, ACT.Copy
                                         ).then_inc(part1_done, 1)
                if name == "transposed":
                    if k == 0:
                        act.wait_ge(mod_a_done, b + 2)
                    wait(act, h_lo_done, count - 1)
                    for c in range(KC):
                        nc.scalar.activation(h_full[:, c, :], dense_ps[:, c, :], ACT.Identity,
                                             bias=mod_front[:, c:c + 1], scale=mod_front[:, 2 + c:3 + c])
                    for c in range(KC):
                        last = nc.scalar.activation(h_hi[:, c, QT * k:QT * (k + 1)], dense_ps[:, c, :],
                                                    ACT.Identity, bias=mod_front[:, c:c + 1],
                                                    scale=mod_front[:, 2 + c:3 + c])
                    last.then_inc(free["transposed"], 1)

            def back(b, s, u):
                q = quarters(b, s)
                if u == 1:
                    act.wait_ge(att_done, b * 2 - (1 if s < 2 else 0))
                    wait(act, ready["out"], q)
                    nc.scalar.activation(o_hi[:], att_n[:, :, QT * s:QT * (s + 1)], ACT.Copy).then_inc(o_hi_done, 1)
                if u == 6:
                    act.wait_ge(ready["norm"], q + 1)
                    if s == 0:
                        act.wait_ge(mod_c_done, b)
                    for c in range(KC):
                        last = nc.scalar.activation(h2[s % 2][:, c, 1:1 + QT], dense_ps[:, c, :], ACT.Identity,
                                                    bias=mod_back[:, c:c + 1], scale=mod_back[:, 2 + c:3 + c])
                    last.then_inc(free["norm"], 1)
                if u == 8:
                    wait(act, ready["key"], q)
                    for m in range(2):
                        act.wait_ge(mixed_done, q * 2 + (m + 1))
                        nc.scalar.activation(mix_hi[:, m], mixed[:, m], ACT.Copy).then_inc(mix_hi_done, 1)
                if u == 10:
                    act.wait_ge(ready["recept"], q + 1)
                    wait(act, free["value"], q)
                    nc.scalar.activation(recept[:], dense_ps[:], ACT.Tanh, scale=0.5).then_inc(free["recept"], 1)
                if u == 11:
                    act.wait_ge(ready["key"], q + 1)
                    nc.scalar.activation(k_relu[:], dense_ps[:], ACT.Relu).then_inc(free["key"], 1)
                    act.wait_ge(free["key"], q + 1)
                    wait(act, ready["value"], q)
                    nc.scalar.activation(k_sq[:], k_relu[:], ACT.Square)
                    nc.scalar.activation(k_hi[:], k_relu[:], ACT.Square).then_inc(k_hi_done, 1)

            def body(b, kind):
                for s, t, at in timeline(b, kind):
                    units = range(COL_FIRST[t], COL_FIRST[t + 1]) if attends(kind) else ()
                    for c in units[:len(units) // 2]:
                        exps(b, s, t, c)
                    for item in at:
                        back(*item)
                    for c in units[len(units) // 2:]:
                        exps(b, s, t, c)
                    if t == 0 and has_late(kind, s):
                        copy_values(*((b - 1, G - 1) if s == 0 else (b, s - 1)), 1)
                    if t == 4 and attends(kind):
                        copy_values(b, s, 0)
                    front(b, kind, s, t)

            pipeline(nc.scalar, body)

        @block.vector
        def _(dve):
            for i in range(2):
                nc.vector.memset(k_stack[i][ROWS:ROWS + MROWS, :, :], 1.0)
            dve.wait_ge(w_hi_done, 1)
            nc.vector.tensor_tensor(w_lo[:], w_raw, w_hi[:].bitcast(F32), ALU.subtract).then_inc(setup_done, 1)
            dve.wait_ge(tanh_done, 1)
            nc.vector.scalar_tensor_tensor(c_silu, c_tanh, 1.0, c_sb, ALU.add, ALU.mult).then_inc(setup_chain, 1)
            dve.wait_ge(setup_chain, 1)
            nc.vector.tensor_scalar(c_silu, c_silu, 0.5, None, ALU.mult).then_inc(silu_done, 1)
            dve.wait_ge(mod_ready, 1)
            mods = mod_t[:].rearrange("p (b i) -> p b i", i=8)
            nc.vector.tensor_copy(mods, col_ps[0][:, 0:8 * B].rearrange("p (i b) -> p b i", b=B)
                                  ).then_inc(setup_chain, 1)
            dve.wait_ge(setup_chain, 2)
            for i in (2, 6):
                last = nc.vector.tensor_scalar(mods[:, :, i:i + 2], mods[:, :, i:i + 2], 1.0, None, ALU.add)
            last.then_inc(setup_done, 1)
            gate_in = dense_flat[0:B, :]
            nc.vector.tensor_copy(gate_val, gate_in).then_inc(setup_chain, 1)
            dve.wait_ge(setup_chain, 3)
            nc.vector.tensor_scalar(gate_abs, gate_val, -1.0, None, ALU.mult).then_inc(setup_chain, 1)
            nc.vector.tensor_scalar(gate_sgn, gate_val, 0.0, 2.0, ALU.is_ge, ALU.mult).then_inc(setup_chain, 1)
            dve.wait_ge(setup_chain, 5)
            nc.vector.tensor_tensor(gate_abs, gate_abs, gate_val, ALU.max).then_inc(setup_chain, 1)
            dve.wait_ge(setup_chain, 6)
            nc.vector.tensor_scalar(gate_abs, gate_abs, 0.25, None, ALU.max).then_inc(setup_chain, 1)
            nc.vector.tensor_scalar(gate_sgn, gate_sgn, -1.0, None, ALU.add).then_inc(setup_chain, 1)
            dve.wait_ge(setup_chain, 8)
            nc.vector.tensor_tensor(gate_val, gate_abs, gate_sgn, ALU.mult).then_inc(setup_chain, 1)
            dve.wait_ge(setup_chain, 9)
            dve.wait_ge(small_loaded, 80)
            nc.vector.tensor_copy(gate_out[:, 0, :], gate_val[:, 0:D])
            nc.vector.tensor_tensor(gate_out[:, 1, :], gate_val[:, 0:D], b_rows, ALU.mult)
            nc.vector.tensor_scalar(gate_out[:, 2, :], gate_val[:, D:2 * D], 0.5, None, ALU.mult
                                    ).then_inc(gates_done, 1)
            nc.vector.memset(zero_col[:], 0.0).then_inc(setup_done, 1)
            dve.wait_ge(setup_done, 3)

            def maximum(b, s, u):
                at = unit_index(b, s, u)
                bank = row_ps[bank_of(UNITS * ((s + 1) % G) + u, UNITS * G)[0]]
                dve.wait_ge(rows_ready, at + 1)
                if u == MT1 or ORDER[u] == "mt0":
                    half = int(u == MT1)
                    wait(dve, max_placed[half], (b * G + (s + 1)) * 48)
                    nc.vector.tensor_copy(max_rows[half][:], bank[:].bitcast(BF16)[0:3 * G, 0:HALF]
                                          ).then_inc(max_done, 1)
                    return
                i, heads, k0, k1, second = ORDER[u]
                dest = (max_b[:, i - 4] if second else max_a[:, i])[:, heads[0]:heads[-1] + 1]
                nc.vector.reduce_max(dest, bank[:, 0:len(heads) * (k1 - k0)].rearrange(
                    "p (h k) -> p h k", h=len(heads)), AX_X).then_inc(max_done, 1)
                if u == FIRST_HALF - 1:
                    split_max(b, s, 0, at + 1)
                if u == MT1 - 1:
                    split_max(b, s, 1, at + 1)

            def split_max(b, s, half, upto):
                chain = b * (7 * G) + (7 * (s + 1) + 3 * half)
                dve.wait_ge(max_done, upto)
                src = max_a[:, 4 * half:4 * half + 4]
                parts = max_parts[half]
                if half:
                    nc.vector.tensor_tensor(src, src, max_b[:], ALU.max).then_inc(max_chain, 1)
                    chain = chain + 1
                    dve.wait_ge(max_chain, chain)
                nc.vector.tensor_scalar(parts[:, :, 0:G], src, -1.0, None, ALU.mult).then_inc(max_chain, 1)
                dve.wait_ge(max_chain, chain + 1)
                nc.vector.scalar_tensor_tensor(max_rest[:], src, -1.0, parts[:, :, 0:G], ALU.mult,
                                               ALU.subtract).then_inc(max_chain, 1)
                dve.wait_ge(max_chain, chain + 2)
                nc.vector.tensor_copy(parts[:, :, G:2 * G], max_rest[:]).then_inc(max_chain, 1)
                dve.wait_ge(max_chain, chain + 3)
                nc.vector.tensor_tensor(parts[:, :, 2 * G:3 * G], max_rest[:], parts[:, :, G:2 * G],
                                        ALU.subtract).then_inc(max_split, 1)

            def layernorm_stats(src, stats, mv, stats_done, mv_done, count):
                for i in range(2):
                    last = nc.vector.bn_stats(stats[:, i, :], src[:, i, :])
                last.then_inc(stats_done, 1)
                wait_apart(dve, "dve", stats_done, count)
                for i in range(2):
                    last = nc.vector.bn_aggr(mv[:, i, :], stats[:, i, :])
                last.then_inc(mv_done, 1)

            def layernorm_apply(src, mv, rstd, dst, rstd_done, done, count):
                dve.wait_ge(rstd_done, count)
                for i in range(2):
                    last = nc.vector.tensor_scalar(dst[:, i, :], src[:, i, :], mv[:, i, 0:1], rstd[:, i:i + 1],
                                                   ALU.subtract, ALU.mult)
                last.then_inc(done, 1)

            def front(b, kind, s, t):
                if not (s == 1 and fronts(kind)):
                    return
                if t == 0:
                    nc.vector.tensor_copy(mod_front[:], mod_t[:, bass.ds(b * 8 + 8, 4)]).then_inc(mod_a_done, 1)
                if t + 1 in T_STEPS:
                    k = T_STEPS.index(t + 1)
                    wait(dve, ready["transposed"], b * 4 + (4 + k))
                    layernorm_apply(xa[:, 2 * k:2 * k + 2, :], mv_a, rstd_a, xn_a, rstd_a_done, xn_a_done,
                                    b * 4 + (4 + k + 1))
                if t + 2 in T_STEPS:
                    k = T_STEPS.index(t + 2)
                    if k == 0:
                        dve.wait_ge(xa_in, b * 16 + 32)
                    layernorm_stats(xa[:, 2 * k:2 * k + 2, :], stats_a, mv_a, stats_a_done, mv_a_done,
                                    b * 4 + (4 + k + 1))

            def rest_of_qk(b, kind, s, t):
                unit = front_unit(b, kind, s, t)
                if unit and unit[0] == "qk":
                    _, k, count = unit
                    side, half = (q_parts, k_parts)[k % 2], k % 4 // 2
                    dve.wait_ge(part1_done, count)
                    wait(dve, parts_done, count - 1)
                    nc.vector.tensor_tensor(qk_rest[:], dense_flat,
                                            side[0][:, HALF * half:HALF * (half + 1)],
                                            ALU.subtract).then_inc(free["qk"], 1)

            def reciprocals(b, half):
                dve.wait_ge(att_placed[half], b * (32 * G) + 32 * G)
                nc.vector.reciprocal(sums[half][:], sums[half][:]).then_inc(recip_done, 1)

            def back(b, s, u):
                q = quarters(b, s)
                xr = residual(b, s)
                if u == 0 and s < 2:
                    dve.wait_ge(recip_in[s], b * 32)
                    wait(dve, o_lo_done, quarters(b, 0) - (2 if s == 0 else 0))
                    cols = slice(HALF * s, HALF * (s + 1))
                    nc.vector.tensor_tensor(att_n[:, :, cols], att[:, :, cols], recips[:], ALU.mult
                                            ).then_inc(att_done, 1)
                if u == 0 and s == 0:
                    nc.vector.tensor_copy(mod_back[:], mod_t[:, bass.ds(b * 8 - 4, 4)]).then_inc(mod_c_done, 1)
                if u == 3:
                    dve.wait_ge(ready["out"], q + 1)
                    ga = gates_att[:, 0:1, :].broadcast_to([P, 2, D])
                    nc.vector.tensor_tensor(gated[:], dense_ps[:], ga, ALU.mult).then_inc(free["out"], 1)
                    dve.wait_ge(free["out"], q + 1)
                    dve.wait_ge(xb_done, q + 1)
                    nc.vector.tensor_tensor(xr, xr, gated[:], ALU.add).then_inc(x1_done, 1)
                if u == 4:
                    dve.wait_ge(x1_done, q + 1)
                    layernorm_stats(xr, stats_c, mv_c, stats_c_done, mv_c_done, q + 1)
                if u == 5:
                    wait(dve, ready["norm"], q)
                    layernorm_apply(xr, mv_c, rstd_c, xn_c, rstd_c_done, xn_c_done, q + 1)
                if u == 7:
                    dve.wait_ge(diff_done, q + 1)
                    wait(dve, mix_lo_done, q * 2)
                    for m in range(2):
                        for c in range(KC):
                            last = nc.vector.scalar_tensor_tensor(
                                mixed[:, m, c, :], h2_diff[:, c, :], mus[:, m, c:c + 1],
                                h2[s % 2][:, c, 0:QT], ALU.mult, ALU.add)
                        last.then_inc(mixed_done, 1)
                if u == 14:
                    dve.wait_ge(ready["value"], q + 1)
                    wait(dve, out_done, q)
                    nc.vector.scalar_tensor_tensor(mix_out[:], recept[:], 1.0, dense_ps[:], ALU.add, ALU.mult
                                                   ).then_inc(free["value"], 1)

            def body(b, kind):
                for s, t, at in timeline(b, kind):
                    units = gaps(t) if has_rows(kind, s) else [[]] * 5
                    if t == 0 and attends(kind):
                        maximum(b, s - 1, MT1)
                    for u in units[0]:
                        maximum(b, s, u)
                    for item in at:
                        back(*item)
                    front(b, kind, s, t)
                    for u in units[1] + units[2] + units[3]:
                        maximum(b, s, u)
                    rest_of_qk(b, kind, s, t)
                    for u in units[4]:
                        maximum(b, s, u)
                    if t == 8 and s == G - 1 and attends(kind):
                        reciprocals(b, 0)
                    if t == 4 and s == 0 and backs(kind):
                        reciprocals(b - 1, 1)

            pipeline(nc.vector, body)

        @block.tensor
        def _(pe):
            pe.wait_ge(silu_done, 1)
            silu = c_silu.rearrange("p (k b) -> p k b", k=KC)
            for i, col in enumerate((0, P, D, D + P, 3 * D, 3 * D + P, 4 * D, 4 * D + P)):
                for c in range(KC):
                    nc.tensor.matmul(col_ps[0][:, B * i:B * (i + 1)], wmod_sb[:, c, col:col + P], silu[:, c, :],
                                     start=(c == 0), stop=(c == KC - 1))
            for i, col in enumerate((2 * D, 5 * D)):
                for c in range(KC):
                    last = nc.tensor.matmul(dense_ps[0:B, i, :], silu[:, c, :], wmod_sb[:, c, col:col + D],
                                            start=(c == 0), stop=(c == KC - 1))
            last.then_inc(mod_ready, 1)
            pe.wait_ge(consts_done, 1)
            pe.wait_ge(setup_done, 3)

            def score_columns(b, s, t, c):
                q0, q1, j = COL_STEPS[t]
                n = COL_HEADS[t]
                if c in (0, COL_FIRST[4]):
                    pe.wait_ge(max_placed[t // 4], b * (48 * G) + 48 * (s + 1))
                bank, ago = bank_of(COLS * s + c, COLS * G)
                wait(pe, exp_done, exp_index(b, s, c) + (1 - ago))
                for i in range(n):
                    h = (c - COL_FIRST[t]) * n + i
                    last = nc.tensor.matmul(col_ps[bank][:, i * (q1 - q0):(i + 1) * (q1 - q0)],
                                            k_stack[s % 2][:, h, P * j:P * (j + 1)],
                                            q_stack[s % 2][:, h, q0:q1], start=(i == 0), stop=(i == n - 1),
                                            skip_group_check=True)
                last.then_inc(cols_ready, 1)

            def row_unit(b, s, u):
                at = unit_index(b, s, u)
                number, ago = bank_of(UNITS * ((s + 1) % G) + u, UNITS * G)
                bank = row_ps[number]
                if u in (0, FIRST_HALF):
                    pe.wait_ge(stack_filled[(s + 1) % 2][int(u > 0)], (b * 2 + ((s + 1) // 2 + 1)) * FILL)
                wait(pe, max_done, at + (1 - ago))
                if u == MT1 or ORDER[u] == "mt0":
                    half = int(u == MT1)
                    pe.wait_ge(max_split, b * (2 * G) + (2 * (s + 1) + half + 1))
                    for i in range(4):
                        last = nc.tensor.transpose(bank[:].bitcast(BF16)[0:3 * G, P * i:P * (i + 1)],
                                                   max_parts[half][:, i, :], ident_bf[:])
                    last.then_inc(rows_ready, 1)
                    return
                i, heads, k0, k1, _ = ORDER[u]
                width = k1 - k0
                stack = (s + 1) % 2
                diagonal = k1 == P * (i + 1)
                for n, h in enumerate(heads):
                    end = n == len(heads) - 1
                    last = nc.tensor.matmul(bank[:, n * width:(n + 1) * width],
                                            q_stack[stack][0:ROWS, h, P * i:P * (i + 1)],
                                            k_stack[stack][0:ROWS, h, k0:k1],
                                            start=(n == 0), stop=(end and not diagonal), skip_group_check=True)
                    if diagonal:
                        last = nc.tensor.matmul(bank[:, (n + 1) * width - P:(n + 1) * width], ident_bf[:],
                                                causal[:], start=False, stop=end, skip_group_check=True)
                last.then_inc(rows_ready, 1)

            def values(b, s, t):
                q0, q1, j = COL_STEPS[t]
                base = 0 if t < 4 else HALF
                if t in DIAGONAL:
                    pe.wait_ge(sel_done, b * (8 * G) + (8 * s + DIAGONAL.index(t) + 1))
                else:
                    pe.wait_ge(exp_done, exp_index(b, s, COL_FIRST[t + 1]))
                if t in (0, 4):
                    wait(pe, val_copied, b * (2 * G) + (2 * s + t // 4))
                if s == 0 and t in (0, 2, 8):
                    pe.wait_ge(free["v"], b * 4 + {0: 1, 2: 2, 8: 4}[t])
                for h in range(G):
                    last = nc.tensor.matmul(val_ps[32 * h:32 * h + 32, q0 - base:q1 - base],
                                            v_ones[:, j, G * s + h].rearrange("p d a -> p (d a)"),
                                            weights[:, t % 2, h, 0:q1 - q0],
                                            start=(j == 0), stop=(q0 == P * j and q1 == q0 + P),
                                            skip_group_check=True)
                last.then_inc(val_done, 1)

            def product(dst, a_hi, a_lo, b_hi, b_lo):
                for c in range(KC):
                    nc.tensor.matmul(dst, a_hi(c), b_hi(c), start=(c == 0), stop=False)
                    nc.tensor.matmul(dst, a_hi(c), b_lo(c), start=False, stop=False)
                    last = nc.tensor.matmul(dst, a_lo(c), b_hi(c), start=False, stop=(c == KC - 1))
                return last

            def w(part, at, n, lo=0, hi=None):
                return lambda c: part[:, at + c * n + lo:at + c * n + (n if hi is None else hi)]

            def qk_unit(chunk, k):
                side, half = k % 2, k // 2
                at = D * side + P * chunk
                cols = slice(HALF * half, HALF * (half + 1))
                return product(dense_flat, w(w_hi, W_QK, 512, at, at + P), w(w_lo, W_QK, 512, at, at + P),
                               lambda c: h_hi[:, c, cols], lambda c: h_lo[:, c, cols])

            def transposes(src):
                for i in range(2):
                    for c in range(KC):
                        last = nc.tensor.transpose(dense_ps[:, c, P * i:P * (i + 1)], src[:, i, P * c:P * (c + 1)],
                                                   ident[:])
                return last

            def tokens_times(a_hi, a_lo, at):
                for i in range(2):
                    cols = slice(P * i, P * (i + 1))
                    last = product(dense_ps[:, i, :], lambda c: a_hi[:, c, cols], lambda c: a_lo[:, c, cols],
                                   w(w_hi, at, D), w(w_lo, at, D))
                return last

            def front(unit):
                name, k, count = unit
                if name == "v":
                    for i in range(2):
                        cols = slice(P * (2 * k + i), P * (2 * k + i + 1))
                        last = product(dense_ps[:, i, :], lambda c: h_hi[:, c, cols], lambda c: h_lo[:, c, cols],
                                       w(w_hi, W_V, D), w(w_lo, W_V, D))
                if name == "qk":
                    if k == 0:
                        pe.wait_ge(h_lo_done, (count - 1) // 2 + 4)
                    last = qk_unit(k // 4, k % 4)
                if name == "transposed":
                    pe.wait_ge(xn_a_done, count)
                    last = transposes(xn_a)
                last.then_inc(ready[name], 1)

            def back(b, s, u):
                unit = back_unit(b, s, u)
                if not unit:
                    return
                name, count = unit
                if name == "out":
                    pe.wait_ge(o_lo_done, count)
                    last = tokens_times(o_hi[:], o_lo[:], W_O)
                if name == "norm":
                    pe.wait_ge(xn_c_done, count)
                    last = transposes(xn_c)
                if name == "recept":
                    pe.wait_ge(mix_lo_done, count * 2 - 1)
                    last = tokens_times(mix_hi[:, 0], mix_lo[:, 0], W_R)
                if name == "key":
                    pe.wait_ge(mix_lo_done, count * 2)
                    for m in range(KC):
                        last = product(dense_ps[:, m, :], w(w_hi, W_K, D, P * m, P * (m + 1)),
                                       w(w_lo, W_K, D, P * m, P * (m + 1)),
                                       lambda c: mix_hi[:, 1, c, :], lambda c: mix_lo[:, 1, c, :])
                if name == "value":
                    pe.wait_ge(k_lo_done, count)
                    last = tokens_times(k_hi[:], k_lo[:], W_F)
                last.then_inc(ready[name], 1)

            def body(b, kind):
                dense = dense_units(b, kind)
                before = [None] if kind == "first" else [dense_units(b - 1, BEFORE[kind])[-1]]

                def claim_dense():
                    if before[0]:
                        pe.wait_ge(free[before[0][2]], before[0][3])
                    before[0] = dense.pop(0)

                for s, t, at in timeline(b, kind):
                    cols = attends(kind)
                    late = (b, s, t - 1) if t else (b - 1, G - 1, STEPS - 1) if s == 0 else (b, s - 1, STEPS - 1)
                    has_values = cols if t else has_late(kind, s)
                    unit = front_unit(b, kind, s, t)
                    backs_now = [item for item in at if back_unit(*item)]
                    work = (4 * cols + 4 * has_values + 6 * bool(unit) + 6 * len(backs_now)) or 1
                    rows = iter(range(sum(PER_STEP[:t]), sum(PER_STEP[:t + 1])) if has_rows(kind, s) else ())
                    total, state = (PER_STEP[t] if has_rows(kind, s) else 0), [0, 0]

                    def rows_after(amount):
                        state[0] += amount
                        while state[1] < min(total, (total * state[0] + work // 2) // work):
                            row_unit(b, s, next(rows))
                            state[1] += 1

                    for c in range(COL_FIRST[t], COL_FIRST[t + 1]) if cols else ():
                        score_columns(b, s, t, c)
                        if t:
                            rows_after(COL_HEADS[t])
                    if t == 0 and cols:
                        row_unit(b, s - 1, MT1)
                        rows_after(4)
                    if has_values:
                        values(*late)
                        rows_after(4)
                    if unit:
                        claim_dense()
                        front(unit)
                        rows_after(6)
                    for item in backs_now:
                        claim_dense()
                        back(*item)
                        rows_after(6)
                    rows_after(work)

            pipeline(nc.tensor, body)


def kernel(**inputs):
    import numpy as np
    import concourse.bacc as bacc
    from concourse.bass_utils import run_bass_kernel_spmd

    w_in = np.asarray(inputs["L0_attn_w_in"])
    by_head = w_in[:2 * D].reshape(2, H // G, G, HD, D).transpose(0, 1, 3, 2, 4).reshape(2 * D, D)
    arrays = {
        "x": np.ascontiguousarray(inputs["L0_attn_inputs"]),
        "w_in_t": np.ascontiguousarray(np.concatenate([by_head, w_in[2 * D:]]).T),
        "w_out_t": np.ascontiguousarray(np.asarray(inputs["L0_attn_w_out"]).T),
        "b_out": np.ascontiguousarray(inputs["L0_attn_b_out"]),
        "w_r_t": np.ascontiguousarray(np.asarray(inputs["L0_ffn_W_r"]).T),
        "w_k_t": np.ascontiguousarray(np.asarray(inputs["L0_ffn_W_k"]).T),
        "w_v_t": np.ascontiguousarray(np.asarray(inputs["L0_ffn_W_v"]).T),
        "mu_r": np.ascontiguousarray(inputs["L0_ffn_mu_r"]),
        "mu_k": np.ascontiguousarray(inputs["L0_ffn_mu_k"]),
        "c_t": np.ascontiguousarray(np.asarray(inputs["L0_c"]).T),
        "wmod": np.ascontiguousarray(inputs["L0_wmod"]),
    }
    nc = bacc.Bacc("TRN2", target_bir_lowering=False, num_devices=1)
    args = [nc.dram_tensor(f"in_{n}", a.shape, F32, kind="ExternalInput").ap() for n, a in arrays.items()]
    out = nc.dram_tensor("out", (B, N, D), F32, kind="ExternalOutput").ap()
    build(nc, *args, out)
    result = run_bass_kernel_spmd(nc, [{f"in_{n}": a for n, a in arrays.items()}], core_ids=[0])
    return result.results[0]["out"]
```
